# Optimizing a Trainium2 kernel written in Bass

```python
import numpy as np
import jax
import jax.numpy as jnp

def _softmax(x, axis=-1):
    return jax.nn.softmax(x, axis=axis)
def _gelu(x):
    return jax.nn.gelu(x, approximate=True)
def _silu(x):
    return jax.nn.silu(x)
def _sigmoid(x):
    return jax.nn.sigmoid(x)
def _layernorm(x, axis=-1, eps=1e-5):
    m = jnp.mean(x, axis=axis, keepdims=True)
    v = jnp.var(x, axis=axis, keepdims=True)
    return (x - m) / jnp.sqrt(v + eps)
def _scatter_add(tgt, idx, src, axis=0):
    return tgt.at[idx].add(src)
def _segment_sum(src, seg, n):
    return jax.ops.segment_sum(src, seg, n)

kernel_name = 'mk_adj_preln_d1_adj_256_38f0bc'

def setup_inputs(seed: int = 0):
    np.random.seed(seed)
    _w = jnp.asarray
    def _rec_inputs():
        import jax
        import jax.numpy as jnp
        _gk = jax.random.key(seed)
        x = -0.000929 + 1 * jax.random.normal(jax.random.fold_in(_gk, 1), (8192, 256), jnp.float32)
        _a = jax.random.bernoulli(jax.random.fold_in(_gk, 2), 0.000976562, (8192, 8192))
        _a = jnp.logical_or(_a, jnp.swapaxes(_a, -1, -2))
        _a = jnp.logical_or(_a, jnp.eye(8192, dtype=bool))
        adj = _a.astype(jnp.int32)
        return x, adj
    x, adj = _rec_inputs()
    def _L0_gnn_setup():
        import jax, jax.numpy as jnp
        import numpy as np
        HEADS = 4
        OUT_DIM = 64
        NEG_SLOPE = 0.2
        key = jax.random.key(seed)
        k1, k2, k3, k4 = jax.random.split(key, 4)
        n, in_dim = (4096, 256)
        x = jax.random.normal(k1, (n, in_dim), dtype=jnp.float32)
        adj = jax.random.randint(k2, (n, n), 0, 2, dtype=jnp.int32)
        W = jax.random.normal(k3, (in_dim, HEADS * OUT_DIM), dtype=jnp.float32) * 0.05
        att = jax.random.normal(k4, (HEADS, 2 * OUT_DIM), dtype=jnp.float32) * 0.05
        return {'x': x, 'adj': adj, 'W': W, 'att': att}
    _L0_gnn_all = _L0_gnn_setup()
    _L0_gnn_in = {k: v for k, v in _L0_gnn_all.items() if k in ('W', 'att', )}
    del _L0_gnn_all

    return {
        "x": x,
        "adj": adj,
        "L0_gnn_W": _L0_gnn_in["W"],
        "L0_gnn_att": _L0_gnn_in["att"],
    }

def reference(x, adj, L0_gnn_W, L0_gnn_att):
    import jax
    import jax.numpy as jnp
    def _L0_gnn_ref(x, adj, W, att):
        import jax, jax.numpy as jnp
        import numpy as np
        HEADS = 4
        OUT_DIM = 64
        NEG_SLOPE = 0.2
        n = x.shape[0]
        h = (x @ W).reshape(n, HEADS, OUT_DIM)
        a_src, a_dst = (att[:, :OUT_DIM], att[:, OUT_DIM:])
        e_src = jnp.einsum('nhd,hd->nh', h, a_src)
        e_dst = jnp.einsum('nhd,hd->nh', h, a_dst)
        scores = e_src[:, None, :] + e_dst[None, :, :]
        scores = jax.nn.leaky_relu(scores, negative_slope=NEG_SLOPE)
        mask = (adj > 0)[:, :, None]
        scores = jnp.where(mask, scores, -jnp.inf)
        alpha = jax.nn.softmax(scores, axis=1)
        h_prime = jnp.einsum('ijh,jhd->ihd', alpha, h)
        return h_prime.reshape(n, HEADS * OUT_DIM)

    h = jnp.maximum(_layernorm(x, axis=-1), 0.0)
    x = x + _L0_gnn_ref(h, adj, L0_gnn_W, L0_gnn_att)
    return x


_drawn_inputs = setup_inputs


def setup_inputs(seed=0):
    import zlib

    import numpy as np

    out = dict(_drawn_inputs(seed))
    spreads = {}
    factors = {'L0_gnn_att': 3.781}
    for name, (base, spread) in spreads.items():
        noise = np.random.default_rng([zlib.crc32(name.encode()), seed]).standard_normal(out[name].shape)
        drawn = base * np.exp(spread * noise) if base else spread * noise
        out[name] = jnp.asarray(drawn.astype(out[name].dtype))
    for name, factor in factors.items():
        out[name] = (out[name] * factor).astype(out[name].dtype)
    return out
```

```python
import concourse.bass as bass
from concourse import mybir
from contextlib import ExitStack



def gat_kernel(nc: bass.Bass, x: bass.AP, adj: bass.AP, W: bass.AP, att: bass.AP, out: bass.AP):
    f32, f16, bf16 = mybir.dt.float32, mybir.dt.float16, mybir.dt.bfloat16
    f8, u8, u16, u32, i32 = (mybir.dt.float8e5, mybir.dt.uint8, mybir.dt.uint16, mybir.dt.uint32,
                             mybir.dt.int32)
    ALU, ACT, AX = mybir.AluOpType, mybir.ActivationFunctionType, mybir.AxisListType

    P = 128
    N, C = x.shape
    H = att.shape[0]
    D = att.shape[1] // 2
    KC = C // P
    WE = C + 2 * H
    PAIR = 2 * P
    NT = N // PAIR
    NR = N // P
    IT = 8
    F = IT * P
    NI = N // F
    G1 = D + 1
    GW = 2 * G1
    DVE_CMP = {True: ((2, 1), (3, 1), (7, 1)), False: ((3, 1), (7, 1))}
    BT = 8
    NB = NT // BT
    SLOTT = 2
    NS = BT // SLOTT
    NC = 4
    XB = SLOTT * 2 * 2 * GW * 2
    METAW = SLOTT * 5
    PKB = XB + 4 * METAW
    CT = 4
    NCH = NT // CT
    HUGE = 2.0 ** 100
    LEAK = 0.2
    EPS = 1e-5
    BITS = 0x78787878
    FLIP = 0x7C7C7C7C

    pack = nc.dram_tensor("pack", [H, NS * NB, P, PKB], u8).ap()
    srow = nc.dram_tensor("srow", [H, N], f32).ap()

    x_t = x.rearrange("(t p b) c -> p t b c", p=P, b=2)
    out_t = out.rearrange("(t p b) c -> p t b c", p=P, b=2)
    adj_t = adj.rearrange("(t p b) j -> p t b j", p=P, b=2)

    ctx = ExitStack()
    with ctx:
        def sb(name, shape, dt):
            return ctx.enter_context(nc.sbuf_tensor(name, shape, dt))

        def sem(name):
            return ctx.enter_context(nc.semaphore(name))

        adjT = sb("adjT", [P, 2, NT, 2 * F], u8)
        raw = sb("raw", [P, 2, IT, PAIR], i32)
        nat = sb("nat", [P, 2, IT, PAIR], u8)
        wslot = sb("wslot", [P, NS, PKB], u8)
        mask = sb("mask", [P, NC, 2, 2 * F], u8)
        srep = sb("srep", [P, 2, F], f32)
        accs = sb("accs", [P, 2 * IT, GW], f32)
        num = sb("num", [P, IT, G1], f32)
        rden = sb("rden", [P, IT], f32)
        osb = sb("osb", [P, IT, C], f32)
        coef = sb("coef", [P, H, NR, 2], f32)
        ident = sb("ident", [P, P], f32)
        identb = sb("identb", [P, P], bf16)
        zerob = sb("zerob", [P, GW], bf16)
        small = sb("small", [P, 32], f32)
        cfs = sb("cfs", [P, 2 * IT], f32)

        hsb = adjT[:, 1, :, :].rearrange("p t f -> p (t f)").bitcast(f32).rearrange(
            "p (r c) -> p r c", c=C)
        scr = mask[:, :, :, :].rearrange("p a b c -> p (a b c)").bitcast(f32)
        hn = scr[:, 0:2 * C].rearrange("p (b c) -> p b c", b=2)
        hnT = scr[:, 2 * C:4 * C].rearrange("p (b c) -> p b c", b=2)
        attb = scr[:, 1024:1536]
        wtmp = scr[:, 1536:2048]
        wsq = scr[:, 2048:2560].rearrange("p (k c) -> p k c", k=KC)
        ones = scr[:, 2560:2688]
        sTs = scr[:, 2688:3200]
        x32 = scr[:, 0:2 * 2 * 2 * CT * G1].rearrange("p (s m r g) -> p s m r g", s=2, m=2, g=G1)
        osc = osb[:, :, :].rearrange("p a b -> p (a b)")
        wext = osc[:, 0:KC * WE].rearrange("p (k c) -> p k c", k=KC)
        meta = osc[:, KC * WE:KC * WE + H * 16 * METAW].rearrange("p (h s w) -> p h s w", h=H, w=METAW)
        stats = osc[:, 1168:1168 + 6 * NR].rearrange("p (r s) -> p r s", s=6)
        mean, var, nmr, tmp, std, rstd = (osc[:, 1552 + NR * k:1552 + NR * (k + 1)] for k in range(6))
        asc = accs[:, :, :].rearrange("p a b -> p (a b)")
        sd = asc[:, 0:2 * H * NR].rearrange("p (k r) -> p k r", k=2 * H)
        vv = asc[:, 512:1024].rearrange("p (m h r) -> p m h r", m=2, h=H)
        gg = asc[:, 1024:1536].rearrange("p (m h r) -> p m h r", m=2, h=H)
        pw = asc[:, 1536:1792]
        pat = asc[:, 1792:1856]
        pat_b = pat.bitcast(f8)
        rawb = raw[:, :, :, :].rearrange("p s i j -> p (s i j)").bitcast(u8)
        packs = [wslot[:, 0:2, :], wslot[:, 2:4, :]] + [
            rawb[:, 2 * PKB * k:2 * PKB * (k + 1)].rearrange("p (k b) -> p k b", k=2) for k in range(2)]
        NPB = len(packs)

        cmax, dmax, negd, neg2d, cg, wn2, wnorm = (small[:, 4 * k:4 * k + 4] for k in range(7))
        eps = small[:, 28:29]

        acc = ctx.enter_context(nc.psum_tensor("acc", [P, 6, 512], f32))
        tp = ctx.enter_context(nc.psum_tensor("tp", [P, 2, F], bf16))

        def group(k):
            return acc[:, k // 3, (k % 3) * GW:(k % 3) * GW + GW]

        w_ld, att_ld = sem("w_ld"), sem("att_ld")
        x_ld = [sem(f"x_ld{k}") for k in range(4)]
        raw_ld = [sem(f"raw_ld{k}") for k in range(2)]
        const_rdy, wext_rdy = sem("const_rdy"), sem("wext_rdy")
        norm_rdy, nmax_rdy, nsq_rdy = sem("norm_rdy"), sem("nmax_rdy"), sem("nsq_rdy")
        stats_rdy, var_rdy, std_rdy, rstd_rdy = sem("stats_rdy"), sem("var_rdy"), sem("std_rdy"), sem("rstd_rdy")
        hn_rdy = sem("hn_rdy")
        hT_ps = sem("hT_ps")
        hT_rdy = sem("hT_rdy")
        h_ps = sem("h_ps")
        h_rdy = sem("h_rdy")
        sd_rdy = sem("sd_rdy")
        nat_rdy = sem("nat_rdy")
        tp_rdy = sem("tp_rdy")
        adjT_rdy = sem("adjT_rdy")
        dseq = sem("dseq")
        dmax_rdy, D_rdy, nD_rdy = sem("dmax_rdy"), sem("D_rdy"), sem("nD_rdy")
        v_rdy, ex_rdy, coef_rdy, g_rdy = sem("v_rdy"), sem("ex_rdy"), sem("coef_rdy"), sem("g_rdy")
        sT_ps, sT_rdy, sT_st = sem("sT_ps"), sem("sT_rdy"), sem("sT_st")
        x32_rdy = sem("x32_rdy")
        den_rdy = sem("den_rdy")
        hi_rdy = sem("hi_rdy")
        lo_rdy = sem("lo_rdy")
        meta_cp = sem("meta_cp")
        pk_st = [sem(f"pk_st{k}") for k in range(NPB)]
        w_slot = [sem(f"w_slot{k}") for k in range(NS)]
        s_ld = [sem("s_ld0"), sem("s_ld1")]
        cmp_act, cmp_dve = sem("cmp_act"), sem("cmp_dve")
        masks_rdy = sem("masks_rdy")
        steps = sem("steps")
        bank_done = sem("bank_done")
        zero_done = sem("zero_done")
        out_rdy = sem("out_rdy")
        num_rdy, rden_rdy, fin, pseq = sem("num_rdy"), sem("rden_rdy"), sem("fin"), sem("pseq")
        x_in, o_st, gate = sem("x_in"), sem("o_st"), sem("gate")

        block = ctx.enter_context(nc.Block())

        def hold(eng, s, v):
            eng.wait_ge(s, v)
            eng.sem_inc(gate, 1)

        def chunk(c4, s):
            return c4 // (NCH // NPB), (c4 % (NCH // NPB)) * (2 * NPB) + 2 * s

        def blocks(eng, body):
            with eng.Fori(0, NI - 1) as ib:
                body(ib, True)
            body(NI - 1, False)

        def heads(eng, ib, at_head, at_body):
            with eng.Fori(0, H // 2) as hp:
                for odd in range(2):
                    g = ib * H + hp * 2 + odd
                    at_head(g, odd)
                    at_body(odd, g, 0, True)
                    with eng.Fori(1, NB) as tb:
                        at_body(odd, g, tb, False)

        @block.sync
        def _(sp):
            sp.dma_start(wext[:, :, 0:C], W.rearrange("(k p) n -> p k n", p=P)).then_inc(w_ld, 16)
            sp.dma_start(attb, att.rearrange("h d -> (h d)").partition_broadcast(P)).then_inc(att_ld, 16)
            for k in range(4):
                r = NR // 4
                sp.dma_start(hsb[:, r * k:r * k + r, :].rearrange("p (t b) c -> p t b c", b=2),
                             x_t[:, r // 2 * k:r // 2 * (k + 1), :, :]).then_inc(x_ld[k], 16)

            def load_raw(m2, s):
                for b in range(2):
                    sp.dma_start(raw[:, s, :, :].rearrange("p (t b) j -> p t b j", b=2)[:, :, b, :],
                                 adj_t[:, bass.ds((m2 // (NT // 2)) * (IT // 2), IT // 2), b,
                                       bass.ds((m2 % (NT // 2)) * (2 * PAIR) + s * PAIR, PAIR)]
                                 ).then_inc(raw_ld[s], 16)

            with sp.Fori(0, NT // 2) as m2:
                for s in range(2):
                    sp.wait_ge(nat_rdy, m2 * 2 + (s + 1))
                    load_raw(m2, s)
            sp.wait_ge(sT_rdy, 1)
            sp.dma_start(srow.rearrange("h (r q) -> r h q", q=P),
                         sTs[0:NR, :].rearrange("r (h q) -> r h q", h=H)).then_inc(sT_st, 16)
            sp.wait_ge(sT_st, 16)
            sp.dma_start(srep[:, 0, :], srow[0, 0:F].partition_broadcast(P)).then_inc(s_ld[0], 16)
            with sp.Fori(0, H * NCH // NPB) as c4:
                for s in range(NPB):
                    hold(sp, hi_rdy, c4 * (2 * NPB) + (2 * s + 6))
                    hold(sp, lo_rdy, c4 * (2 * NPB) + (2 * s + 6))
                    hold(sp, meta_cp, c4 * NPB + (s + 1))
                    h, first_slot = chunk(c4, s)
                    sp.dma_start(pack[h, bass.ds(first_slot, 2), :, :].rearrange("k p b -> p k b"),
                                 packs[s]).then_inc(pk_st[s], 16)
            for s in range(NPB):
                sp.wait_ge(pk_st[s], 16 * (H * NCH // NPB + 1))
            for s in range(NS):
                sp.dma_start(wslot[:, s, :], pack[0, s, :, :]).then_inc(w_slot[s], 16)
            for s in range(2):
                load_raw(NT // 2, s)

            def body(ib, prep):
                def at_head(g, odd):
                    nxt = (g + 1) % (NI * H)
                    hold(sp, steps, g * NT + NC)
                    sp.dma_start(srep[:, 1 - odd, :],
                                 srow[nxt % H, bass.ds((nxt // H) * F, F)].partition_broadcast(P)
                                 ).then_inc(s_ld[1 - odd], 16)

                def at_body(odd, g, tb, first):
                    n = g * NB + tb

                    def more(s):
                        if prep:
                            hold(sp, nat_rdy, n * 2 + (NT + s + 3))
                            load_raw((n + (NT // 2 + 1)) % (NI * NT // 2), s)

                    def refill(s):
                        nxt = n + 1
                        hold(sp, steps, n * BT + (SLOTT * (s + 1) + NC))
                        sp.dma_start(wslot[:, s, :], pack[(nxt // NB) % H, (nxt % NB) * NS + s, :, :]
                                     ).then_inc(w_slot[s], 16)

                    more(0)
                    refill(0)
                    refill(1)
                    more(1)
                    refill(2)
                    refill(3)

                heads(sp, ib, at_head, at_body)

            blocks(sp, body)
            for s in range(NS):
                sp.wait_ge(w_slot[s], 16 * (NI * H * NB + 1))
            for s in range(2):
                sp.wait_ge(raw_ld[s], 32 * (NI * NT // 2 + 1))
            sp.wait_ge(s_ld[0], 16 * (NI * H // 2 + 1))

        @block.gpsimd
        def _(pool):
            pool.memset(ident[:, :], 0.0).then_inc(pseq, 1)
            pool.memset(identb[:, :], 0.0).then_inc(pseq, 1)
            pool.memset(zerob[:, :], 0.0).then_inc(const_rdy, 1)
            pool.memset(ones, 1.0).then_inc(const_rdy, 1)
            pool.memset(num[:, :, :], 1.0).then_inc(const_rdy, 1)
            pool.wait_ge(pseq, 2)
            pool.affine_select(out=ident[:, :], in_=ident[:, :], compare_op=ALU.not_equal, fill=1.0, base=0,
                               pattern=[[-1, P]], channel_multiplier=1).then_inc(const_rdy, 1)
            pool.affine_select(out=identb[:, :], in_=identb[:, :], compare_op=ALU.not_equal, fill=1.0, base=0,
                               pattern=[[-1, P]], channel_multiplier=1).then_inc(const_rdy, 1)
            pool.wait_ge(dmax_rdy, 1)
            pool.partition_all_reduce(dmax, cmax, P, bass.bass_isa.ReduceOp.max).then_inc(D_rdy, 1)
            pool.wait_ge(g_rdy, 1)
            pool.wait_ge(h_rdy, NR + 2)
            with pool.Fori(0, H * NCH // NPB) as c4:
                for s in range(NPB):
                    h, first_slot = chunk(c4, s)
                    r = first_slot * (2 * SLOTT)
                    hold(pool, hi_rdy, c4 * (2 * NPB) + (2 * s + 2))
                    hold(pool, lo_rdy, c4 * (2 * NPB) + (2 * s + 2))
                    pool.tensor_tensor(
                        x32[:, s % 2, :, :, 0:D],
                        hsb[:, bass.ds(r, 2 * CT), bass.ds(h * D, D)].unsqueeze(1)
                        .broadcast_to([P, 2, 2 * CT, D]),
                        gg[:, :, h, bass.ds(r, 2 * CT)].unsqueeze(3).broadcast_to([P, 2, 2 * CT, D]),
                        ALU.mult).then_inc(x32_rdy, 1)
                    hold(pool, pk_st[s], c4 * 16 + 16)
                    pool.tensor_copy(packs[s][:, :, XB:PKB].bitcast(u32),
                                     meta[:, h, bass.ds(first_slot, 2), :].bitcast(u32)).then_inc(meta_cp, 1)
            pool.wait_ge(meta_cp, H * NCH)
            pool.wait_ge(coef_rdy, 2)

            own = 2

            with pool.Fori(0, NI) as ib:
                pool.dma_start(osb[:, :, :].rearrange("p (t b) c -> p t b c", b=2),
                               x_t[:, bass.ds(ib * (IT // 2), IT // 2), :, :]).then_inc(x_in, 16)
                for h in range(H):
                    g = ib * H + h
                    pool.tensor_copy(cfs[:, :], coef[:, h, bass.ds(ib * IT, IT), :]
                                     .rearrange("p r m -> p (r m)")).then_inc(pseq, 1)
                    pool.wait_ge(out_rdy, g * 6 + 12)
                    pool.tensor_tensor(accs[:, :, 0:G1], accs[:, :, 0:G1], accs[:, :, G1:GW],
                                       ALU.add).then_inc(pseq, 1)
                    pool.wait_ge(pseq, g * 4 + (own + 2))
                    pool.tensor_tensor(accs[:, :, 0:G1], accs[:, :, 0:G1],
                                       cfs[:, :].unsqueeze(2).broadcast_to([P, 2 * IT, G1]),
                                       ALU.mult).then_inc(pseq, 1)
                    pool.wait_ge(pseq, g * 4 + (own + 3))
                    pool.wait_ge(rden_rdy, g + 2)
                    pm = accs[:, :, 0:G1].rearrange("p (r m) g -> p r m g", m=2)
                    pool.tensor_tensor(num[:, :, :], pm[:, :, 0, :], pm[:, :, 1, :], ALU.add).then_inc(num_rdy, 1)
                    pool.wait_ge(rden_rdy, g + 3)
                    pool.tensor_tensor(num[:, :, 0:D], num[:, :, 0:D],
                                       rden[:, :].unsqueeze(2).broadcast_to([P, IT, D]),
                                       ALU.mult).then_inc(pseq, 1)
                    pool.wait_ge(pseq, g * 4 + (own + 4))
                    pool.wait_ge(x_in, ib * 16 + 16)
                    pool.tensor_tensor(osb[:, :, h * D:(h + 1) * D], osb[:, :, h * D:(h + 1) * D],
                                       num[:, :, 0:D], ALU.add).then_inc(fin, 1)
                hold(pool, fin, ib * H + H)
                pool.dma_start(out_t[:, bass.ds(ib * (IT // 2), IT // 2), :, :],
                               osb[:, :, :].rearrange("p (t b) c -> p t b c", b=2)).then_inc(o_st, 16)
                hold(pool, o_st, ib * 16 + 16)

        @block.scalar
        def _(act):
            act.wait_ge(nmax_rdy, 1)
            act.activation(wnorm, wn2, ACT.Sqrt, scale=float(C)).then_inc(nsq_rdy, 1)
            act.wait_ge(var_rdy, 1)
            act.activation(std, var, ACT.Sqrt).then_inc(std_rdy, 1)
            act.wait_ge(rstd_rdy, 1)

            def normalise(r, b):
                hold(act, hT_ps, r + 1)
                act.activation(hn[:, b, :], hsb[:, r, :], ACT.Relu, bias=nmr[:, bass.ds(r, 1)],
                               scale=rstd[:, bass.ds(r, 1)]).then_inc(hn_rdy, 1)

            def store_h(r, b):
                hold(act, h_ps, r + 3)
                act.activation(hsb[:, r, :], acc[:, 2 + b, 0:C], ACT.Copy).then_inc(h_rdy, 1)
                act.activation(sd[:, :, r], acc[:, 2 + b, C:WE], ACT.Copy).then_inc(sd_rdy, 1)

            for b in range(2):
                normalise(b, b)
            with act.Fori(0, NT - 1) as t:
                for b in range(2):
                    normalise(t * 2 + (2 + b), b)
                    store_h(t * 2 + b, b)
            for b in range(2):
                store_h(NR - 2 + b, b)
            act.wait_ge(nD_rdy, 2)
            for h in range(H):
                act.activation(vv[:, 0, h, :], sd[:, H + h, :], ACT.Exp, bias=negd[:, h:h + 1]).then_inc(v_rdy, 1)
                act.activation(vv[:, 1, h, :], sd[:, H + h, :], ACT.Exp, bias=neg2d[:, h:h + 1],
                               scale=LEAK).then_inc(v_rdy, 1)
            act.wait_ge(ex_rdy, 2)
            cf = coef[:, :, :, :].rearrange("p h r m -> p (h r m)")
            act.activation(cf, cf, ACT.Exp).then_inc(coef_rdy, 1)
            with act.Fori(0, H * NCH // NPB) as c4:
                for s in range(NPB):
                    act.wait_ge(pk_st[s], c4 * 16 + 16)
                    act.wait_ge(x32_rdy, c4 * NPB + (s + 1))
                    act.wait_ge(den_rdy, c4 * NPB + (s + 1))
                    for m in range(2):
                        hi = packs[s][:, :, 0:XB].bitcast(f16).rearrange(
                            "p k (r m g) -> p k r m g", m=2, g=GW)[:, :, :, m, 0:G1]
                        act.activation(hi, x32[:, s % 2, m, :, :].rearrange("p (k r) g -> p k r g", k=2),
                                       ACT.Copy).then_inc(hi_rdy, 1)

            def body(ib, prep):
                def at_head(g, odd):
                    hold(act, s_ld[odd], (g // 2) * 16 + 16)

                def at_body(odd, g, tb, first):
                    n = g * NB + tb
                    for tt in range(BT):
                        s, k = tt // SLOTT, tt % SLOTT
                        kd = wslot[:, s, XB:PKB].bitcast(f32)
                        if k == 0:
                            hold(act, w_slot[s], n * 16 + 16)
                        hold(act, steps, n * BT + (tt + 1))
                        cm = mask[:, tt % NC, 0, :].rearrange("p (f b) -> p f b", b=2)
                        for b in range(2):
                            if (tt, b) not in DVE_CMP[first]:
                                ins = act.activation(cm[:, :, b].bitcast(f8), srep[:, odd, :], ACT.Relu,
                                                     bias=kd[:, 2 * k + b:2 * k + b + 1], scale=HUGE,
                                                     saturate=False)
                        ins.then_inc(cmp_act, 1)
                        if first and tt == 1:
                            sums_out(g)

                heads(act, ib, at_head, at_body)

            def sums_out(g):
                act.wait_ge(num_rdy, g + 1)
                for k in range(6):
                    if k < 5:
                        act.wait_ge(bank_done, g * (5 * NB) + (k + 1))
                    else:
                        act.wait_ge(steps, g * NT + NC)
                    m = min(3, 2 * IT - 3 * k)
                    act.activation(accs[:, 3 * k:3 * k + m, :],
                                   acc[:, k, 0:m * GW].rearrange("p (a g) -> p a g", a=m),
                                   ACT.Copy).then_inc(out_rdy, 1)

            act.wait_ge(zero_done, 1)
            blocks(act, body)
            sums_out(NI * H)

        @block.vector
        def _(dve):
            own = [0]

            def link(ins):
                own[0] += 1
                ins.then_inc(dseq, 1)
                dve.wait_ge(dseq, own[0])

            dve.memset(eps, EPS)
            dve.wait_ge(w_ld, 16)
            dve.wait_ge(att_ld, 16)
            wt4 = wtmp.rearrange("p (h s d) -> p h s d", h=H, s=2)
            at4 = attb.rearrange("p (h s d) -> p h s d", h=H, s=2)
            for k in range(KC):
                wk = wext[:, k, 0:C].rearrange("p (h d) -> p h d", h=H)
                link(dve.tensor_tensor(wt4, wk.unsqueeze(2).broadcast_to([P, H, 2, D]), at4, ALU.mult))
                ins = dve.tensor_reduce(wext[:, k, C:WE].rearrange("p (s h) -> p h s", s=2), wt4, AX.X, ALU.add)
                ins.then_inc(wext_rdy, 1)
                dve.wait_ge(wext_rdy, k + 1)
            dve.tensor_tensor(wsq, wext[:, :, 0:C], wext[:, :, 0:C], ALU.mult).then_inc(wext_rdy, 1)
            dve.wait_ge(norm_rdy, 1)
            dve.tensor_reduce(wn2, acc[:, 5, 0:C].rearrange("p (h d) -> p h d", h=H), AX.X,
                              ALU.max).then_inc(nmax_rdy, 1)
            for k in range(4):
                dve.wait_ge(x_ld[k], 16)
                with dve.Fori(0, NR // 16) as r4:
                    for u in range(4):
                        r = r4 * 4 + (NR // 4 * k + u)
                        dve.bn_stats(stats[:, r, :], hsb[:, r, :]).then_inc(stats_rdy, 1)
            dve.wait_ge(stats_rdy, NR)
            me, ve, mo, vo = (stats[:, :, c] for c in (1, 2, 4, 5))
            dve.tensor_tensor(mean, me, mo, ALU.add)
            link(dve.tensor_tensor(tmp, me, mo, ALU.subtract))
            link(dve.tensor_tensor(tmp, tmp, tmp, ALU.mult))
            link(dve.tensor_tensor(var, ve, vo, ALU.add))
            link(dve.scalar_tensor_tensor(out=var, in0=tmp, scalar=C / 4.0, in1=var, op0=ALU.mult, op1=ALU.add))
            dve.tensor_scalar(var, var, 1.0 / C, EPS, ALU.mult, ALU.add).then_inc(var_rdy, 1)
            dve.wait_ge(var_rdy, 1)
            dve.wait_ge(std_rdy, 1)
            link(dve.reciprocal(rstd, std))
            link(dve.tensor_tensor(tmp, rstd, rstd, ALU.mult))
            link(dve.tensor_tensor(tmp, tmp, var, ALU.mult))
            link(dve.tensor_scalar(tmp, tmp, -0.5, 1.5, ALU.mult, ALU.add))
            link(dve.tensor_tensor(rstd, rstd, tmp, ALU.mult))
            dve.scalar_tensor_tensor(out=nmr, in0=mean, scalar=-0.5, in1=rstd, op0=ALU.mult,
                                     op1=ALU.mult).then_inc(rstd_rdy, 1)

            def convert(m2, s):
                dve.wait_ge(raw_ld[s], m2 * 32 + 32)
                dve.wait_ge(tp_rdy, m2 * 2 + (s + 1))
                dve.tensor_scalar(nat[:, s, :, :], raw[:, s, :, :], 0.0, float(0x3C), ALU.is_gt,
                                  ALU.mult).then_inc(nat_rdy, 1)

            def store_T(m2, s):
                dve.wait_ge(tp_rdy, m2 * 2 + (s + 3))
                dve.tensor_scalar(adjT[:, (m2 // (NT // 2)) % 2, (m2 % (NT // 2)) * 2 + s, :].bitcast(u16),
                                  tp[:, s, :].bitcast(u16), 1, None,
                                  ALU.logical_shift_left).then_inc(adjT_rdy, 1)

            def copy_hT(r, b):
                dve.wait_ge(hT_ps, r + 3)
                dve.wait_ge(h_ps, r + 1)
                dve.tensor_copy(hnT[:, b, :], acc[:, b, 0:C]).then_inc(hT_rdy, 1)

            def project(t2, last):
                for u in range(2):
                    r = t2 * 4 + 2 * u
                    copy_hT(r + 1, 1)
                    convert(t2, u)
                    if not (last and u == 1):
                        copy_hT(r + 2, 0)
                    store_T(t2, u)

            copy_hT(0, 0)
            with dve.Fori(0, NT // 2 - 1) as t2:
                project(t2, False)
            project(NT // 2 - 1, True)
            dve.wait_ge(sd_rdy, NR + 2)
            dve.tensor_reduce(cmax, sd[:, H:2 * H, :], AX.X, ALU.max).then_inc(dmax_rdy, 1)
            dve.wait_ge(sT_ps, 1)
            dve.tensor_copy(sTs[0:NR, :], acc[0:NR, 4, 0:H * P]).then_inc(sT_rdy, 1)
            dve.wait_ge(nsq_rdy, 1)
            link(dve.tensor_scalar(cg, wnorm, 1.0, None, ALU.max))
            link(dve.reciprocal(cg, cg))
            dve.wait_ge(D_rdy, 1)
            dve.tensor_scalar(negd, dmax, -1.0, None, ALU.mult).then_inc(nD_rdy, 1)
            dve.tensor_scalar(neg2d, dmax, -LEAK, None, ALU.mult).then_inc(nD_rdy, 1)
            for h in range(H):
                ins = dve.tensor_scalar(coef[:, h, :, 0], sd[:, h, :], dmax[:, h:h + 1], 1.0 - LEAK,
                                        ALU.add, ALU.mult)
            link(ins)
            dve.tensor_scalar(coef[:, :, :, 1], coef[:, :, :, 0], -1.0, 0.0, ALU.mult, ALU.min).then_inc(ex_rdy, 1)
            dve.wait_ge(ex_rdy, 1)
            dve.tensor_scalar(coef[:, :, :, 0], coef[:, :, :, 0], 0.0, None, ALU.min).then_inc(ex_rdy, 1)
            dve.wait_ge(v_rdy, 2 * H)
            v0 = vv[:, 0, :, :].rearrange("p h r -> p (h r)")
            link(dve.tensor_scalar(pat_b, v0, 2.0 ** -28, 2.0 ** 15, ALU.max, ALU.mult, saturate=False))
            link(dve.tensor_scalar(pat.bitcast(u32), pat.bitcast(u32), BITS, None, ALU.bitwise_and))
            link(dve.tensor_copy(pw, pat_b))
            link(dve.reciprocal(pw, pw))
            for h in range(H):
                dve.tensor_scalar(gg[:, 0, h, :], vv[:, 0, h, :], cg[:, h:h + 1], 2.0 ** 28, ALU.mult, ALU.mult)
                ins = dve.tensor_scalar(gg[:, 1, h, :], vv[:, 1, h, :], cg[:, h:h + 1], 2.0 ** 15,
                                        ALU.mult, ALU.mult)
            link(ins)
            g0 = gg[:, 0, :, :].rearrange("p h r -> p (h r)")
            link(dve.tensor_tensor(g0, g0, pw, ALU.mult))
            hs = meta.rearrange("p h s w -> p (h s) w")
            dd = sd[:, H:2 * H, :].rearrange("p h (s w) -> p (h s) w", w=2 * SLOTT)
            w4 = 2 * SLOTT
            dve.tensor_scalar(hs[:, :, 0:w4], dd, HUGE, None, ALU.mult)
            dve.tensor_scalar(hs[:, :, w4:2 * w4], dd, -1.0, None, ALU.mult)
            link(dve.tensor_copy(hs[:, :, 2 * w4:METAW].bitcast(u16).rearrange("p s (k c) -> p s k c", c=2),
                                 pat.bitcast(u16).rearrange("p (s k) -> p s k", k=SLOTT).unsqueeze(3)
                                 .broadcast_to([P, H * NS * NB, SLOTT, 2])))
            dve.wait_ge(coef_rdy, 1)
            dve.tensor_scalar(coef[:, :, :, 0], coef[:, :, :, 0], 4.0, None, ALU.mult).then_inc(coef_rdy, 1)
            dve.nop().then_inc(g_rdy, 1)
            with dve.Fori(0, H * NCH // NPB) as c4:
                def den_column(s):
                    h, first_slot = chunk(c4, s)
                    dve.wait_ge(hi_rdy, c4 * (2 * NPB) + (2 * s + 2))
                    dve.wait_ge(lo_rdy, c4 * (2 * NPB) + (2 * s + 2))
                    dve.tensor_copy(x32[:, s % 2, :, :, D],
                                    gg[:, :, h, bass.ds(first_slot * (2 * SLOTT), 2 * CT)]).then_inc(den_rdy, 1)

                def low_parts(s):
                    dve.wait_ge(x32_rdy, c4 * NPB + (s + 1))
                    dve.wait_ge(den_rdy, c4 * NPB + (s + 1))
                    for m in range(2):
                        dve.wait_ge(hi_rdy, c4 * (2 * NPB) + (2 * s + m + 5))
                        parts = packs[s][:, :, 0:XB].bitcast(f16).rearrange(
                            "p k (r m g) -> p k r m g", m=2, g=GW)[:, :, :, m, :]
                        dve.tensor_tensor(parts[:, :, :, G1:GW],
                                          x32[:, s % 2, m, :, :].rearrange("p (k r) g -> p k r g", k=2),
                                          parts[:, :, :, 0:G1], ALU.subtract).then_inc(lo_rdy, 1)

                den_column(0)
                den_column(1)
                for s in range(NPB):
                    low_parts(s)
                    if s + 2 < NPB:
                        den_column(s + 2)

            def body(ib, prep):
                def at_body(odd, g, tb, first):
                    n = g * NB + tb
                    own = len(DVE_CMP[False])
                    cmps = n * own + g if first else n * own + g + 1
                    for tt in range(BT):
                        s, k, sl = tt // SLOTT, tt % SLOTT, tt % NC
                        words = wslot[:, s, XB:PKB]
                        cm = mask[:, sl, 0, :].rearrange("p (f b) -> p f b", b=2)
                        for b in range(2):
                            if (tt, b) in DVE_CMP[first]:
                                dve.wait_ge(w_slot[s], n * 16 + 16)
                                dve.wait_ge(steps, n * BT + (tt + 1))
                                j = w4 + 2 * k + b
                                dve.tensor_scalar(cm[:, :, b], srep[:, odd, :],
                                                  words.bitcast(f32)[:, j:j + 1], float(0x7C),
                                                  ALU.is_gt, ALU.mult).then_inc(cmp_dve, 1)
                        dve.wait_ge(cmp_act, n * BT + (tt + 1))
                        if any(c[0] == tt for c in DVE_CMP[first]):
                            dve.wait_ge(cmp_dve, cmps + sum(1 for c in DVE_CMP[first] if c[0] <= tt))
                        plus = mask[:, sl, 0, :].bitcast(u32)
                        minus = mask[:, sl, 1, :].bitcast(u32)
                        edges = adjT[:, ib % 2, tb * BT + tt, :].bitcast(u32)
                        dve.scalar_tensor_tensor(out=minus, in0=plus, scalar=FLIP, in1=edges,
                                                 op0=ALU.bitwise_xor, op1=ALU.bitwise_and)
                        j = 2 * w4 + k
                        dve.scalar_tensor_tensor(out=plus, in0=plus, scalar=words.bitcast(u32)[:, j:j + 1],
                                                 in1=edges, op0=ALU.bitwise_and,
                                                 op1=ALU.bitwise_and).then_inc(masks_rdy, 1)
                        if prep:
                            if tt % 4 == 1:
                                convert(n + NT // 2, tt // 4)
                            if tt % 4 == 3:
                                store_T(n + NT // 2, tt // 4)
                        if first and tt == 1:
                            denominators(g)

                def at_head(g, odd):
                    hold(dve, s_ld[odd], (g // 2) * 16 + 16)
                    hold(dve, adjT_rdy, ib * NT + (NT + 2))

                heads(dve, ib, at_head, at_body)

            def denominators(g):
                dve.wait_ge(num_rdy, g + 1)
                dve.reciprocal(rden[:, :], num[:, :, D]).then_inc(rden_rdy, 1)

            dve.wait_ge(const_rdy, 5)
            blocks(dve, body)
            denominators(NI * H)
            denominators(NI * H + 1)

        @block.tensor
        def _(pe):
            for s in (hT_ps, h_ps, tp_rdy):
                pe.sem_inc(s, 2)
            pe.sem_inc(steps, NC)
            for s in (hT_rdy, h_rdy, sd_rdy, nat_rdy, adjT_rdy):
                pe.sem_inc(s, 2)
            for s in (hi_rdy, lo_rdy):
                pe.sem_inc(s, 4)
            pe.sem_inc(num_rdy, 2)
            for s in pk_st:
                pe.sem_inc(s, 16)
            pe.wait_ge(const_rdy, 5)
            pe.wait_ge(wext_rdy, KC + 1)
            for k in range(KC):
                ins = pe.matmul(acc[:, 5, 0:C], ones, wsq[:, k, :], start=(k == 0), stop=(k == KC - 1))
            ins.then_inc(norm_rdy, 1)

            def transpose_adj(m2, s):
                pe.wait_ge(nat_rdy, m2 * 2 + (s + 3))
                pe.wait_ge(adjT_rdy, m2 * 2 + (s + 1))
                for i in range(IT):
                    ins = pe.transpose(tp[:, s, i * P:(i + 1) * P], nat[:, s, i, :].bitcast(bf16), identb[:, :])
                ins.then_inc(tp_rdy, 1)

            def transpose_row(r, b):
                pe.wait_ge(hn_rdy, r + 1)
                pe.wait_ge(hT_rdy, r + 1)
                for k in range(KC):
                    ins = pe.transpose(acc[:, b, k * P:(k + 1) * P], hn[:, b, k * P:(k + 1) * P], ident[:, :])
                ins.then_inc(hT_ps, 1)

            def project(t2, last):
                for u in range(2):
                    r = t2 * 4 + 2 * u
                    for b in range(2):
                        if not (last and u == 1 and b == 1):
                            transpose_row(r + (b + 1), 1 - b)
                        pe.wait_ge(hT_rdy, r + (b + 3))
                        pe.wait_ge(h_rdy, r + (b + 1))
                        pe.wait_ge(sd_rdy, r + (b + 1))
                        for k in range(KC):
                            ins = pe.matmul(acc[:, 2 + b, 0:WE], hnT[:, b, k * P:(k + 1) * P], wext[:, k, :],
                                            start=(k == 0), stop=(k == KC - 1))
                        ins.then_inc(h_ps, 1)
                        if b == 0:
                            transpose_adj(t2, u)

            transpose_row(0, 0)
            with pe.Fori(0, NT // 2 - 1) as t2:
                project(t2, False)
            project(NT // 2 - 1, True)
            pe.wait_ge(sd_rdy, NR + 2)
            pe.wait_ge(h_rdy, NR + 2)
            for h in range(H):
                ins = pe.transpose(acc[0:NR, 4, h * P:(h + 1) * P], sd[:, h, :], ident[:, :])
            ins.then_inc(sT_ps, 1)
            pe.wait_ge(sT_rdy, 1)
            for i in range(2 * IT):
                ins = pe.matmul(group(i), zerob[:, 0:P], zerob[:, :], start=(i % 3 == 0), stop=False,
                                skip_group_check=True)
                if i % 3 == 2:
                    ins.then_inc(bank_done, 1)
            ins.then_inc(zero_done, 1)

            def body(ib, prep):
                def at_body(odd, g, tb, first):
                    n = g * NB + tb
                    for tt in range(BT):
                        s, k, sl = tt // SLOTT, tt % SLOTT, tt % NC
                        hold(pe, masks_rdy, n * BT + (tt + 1))
                        if k == 0:
                            hold(pe, w_slot[s], n * 16 + 16)
                        wts = wslot[:, s, 0:XB].bitcast(f16).rearrange("p (r m g) -> p r m g", m=2, g=GW)
                        for bank in range(6):
                            if first and tt == 0:
                                hold(pe, out_rdy, g * 6 + (bank + 1))
                                pe.matmul(acc[:, bank, 0:1], zerob[:, 0:P], zerob[:, 0:1], start=True,
                                          stop=False, skip_group_check=True)
                            for b in range(2):
                                for i in range(3 * bank, min(3 * bank + 3, 2 * IT)):
                                    m = i % 2
                                    mk = mask[:, sl, m, :].rearrange("p (f b) -> p f b", b=2)
                                    rows = mk[:, (i // 2) * P:(i // 2 + 1) * P, b].bitcast(f8)
                                    ins = pe.matmul(group(i), rows, wts[:, 2 * k + b, m, :], start=False,
                                                    stop=False, skip_group_check=True)
                            if tt == BT - 1 and bank < 5:
                                ins.then_inc(bank_done, 1)
                        ins.then_inc(steps, 1)
                        if prep and tt % 4 == 1:
                            transpose_adj(n + NT // 2, tt // 4)

                heads(pe, ib, lambda g, odd: None, at_body)

            blocks(pe, body)


def kernel(**inputs):
    import numpy as _np
    import concourse.bacc as _bacc
    from concourse import mybir as _mybir
    from concourse.bass_utils import run_bass_kernel_spmd as _run

    nc = _bacc.Bacc("TRN2", target_bir_lowering=False, num_devices=1)
    arrays, args = {}, []
    for name in ('x', 'adj', 'L0_gnn_W', 'L0_gnn_att'):
        a = _np.ascontiguousarray(inputs[name])
        arrays[f"in_{name}_dram"] = a
        args.append(nc.dram_tensor(f"in_{name}_dram", a.shape, _mybir.dt.from_np(a.dtype), kind="ExternalInput").ap())
    o = nc.dram_tensor("out_0_dram", inputs['x'].shape, _mybir.dt.float32, kind="ExternalOutput").ap()
    gat_kernel(nc, *args, o)
    r = _run(nc, [arrays], core_ids=[0])
    return r.results[0]["out_0_dram"]
```
